# Optimizing a Trainium2 kernel written in Bass

```python
import numpy as np
import jax
import jax.numpy as jnp

def _softmax(x, axis=-1):
    return jax.nn.softmax(x, axis=axis)

def _gelu(x):
    return jax.nn.gelu(x, approximate=True)

def _silu(x):
    return jax.nn.silu(x)

def _sigmoid(x):
    return jax.nn.sigmoid(x)

def _layernorm(x, axis=-1, eps=1e-05):
    m = jnp.mean(x, axis=axis, keepdims=True)
    v = jnp.var(x, axis=axis, keepdims=True)
    return (x - m) / jnp.sqrt(v + eps)

def _scatter_add(tgt, idx, src, axis=0):
    return tgt.at[idx].add(src)

def _segment_sum(src, seg, n):
    return jax.ops.segment_sum(src, seg, n)
kernel_name = 'mk_rec_standalone_d1_rec_r8_cf6735'

def setup_inputs(seed: int=0):
    np.random.seed(seed)
    _w = jnp.asarray

    def _rec_inputs():
        import jax
        import jax.numpy as jnp
        _rk = jax.random.key(seed)
        r_sparse_embed = -0.000928989 + 1.00043 * jax.random.normal(jax.random.fold_in(_rk, 1), (512, 32, 16), jnp.float32)
        return r_sparse_embed
    r_sparse_embed = _rec_inputs()

    def _L0_rec_setup():
        import jax, jax.numpy as jnp
        import numpy as np
        NUM_FIELD = 32
        EMBED_DIM = 16
        BATCH = 256

        def _cin(x0, conv_params, split_flags):
            B, _, D = x0.shape
            x = x0
            results = []
            for (W, b), split in zip(conv_params, split_flags):
                h = x.shape[1]
                z = jnp.einsum('bhd,bmd->bhmd', x, x0).reshape(B, h * x0.shape[1], D)
                xk = jax.nn.relu(jnp.einsum('oc,bcd->bod', W, z) + b[None, :, None])
                if split:
                    half = xk.shape[1] // 2
                    x, xk = (xk[:, :half], xk[:, half:])
                else:
                    x = xk
                results.append(xk)
            return jnp.sum(jnp.concatenate(results, axis=1), axis=2)
        key = jax.random.key(seed)
        ks = jax.random.split(key, 6)

        def xavier(k, shape):
            fan_in, fan_out = (shape[1], shape[0])
            lim = np.sqrt(6.0 / (fan_in + fan_out))
            return jax.random.uniform(k, shape, jnp.float32, -lim, lim)
        sparse_embed = jax.random.normal(ks[0], (BATCH, NUM_FIELD, EMBED_DIM), jnp.float32)
        W1 = xavier(ks[1], (128, NUM_FIELD * 32))
        W2 = xavier(ks[2], (128, NUM_FIELD * 64))
        W3 = xavier(ks[3], (128, NUM_FIELD * 64))
        Wo = jax.random.normal(ks[4], (1, 256), jnp.float32) * np.sqrt(2.0 / (256 + 1))
        return {'sparse_embed': sparse_embed, 'W1': W1, 'b1': jnp.zeros((128,), jnp.float32), 'W2': W2, 'b2': jnp.zeros((128,), jnp.float32), 'W3': W3, 'b3': jnp.zeros((128,), jnp.float32), 'Wo': Wo, 'bo': jnp.zeros((1,), jnp.float32)}
    _L0_rec_all = _L0_rec_setup()
    _L0_rec_in = {k: v for k, v in _L0_rec_all.items() if k in ('W1', 'b1', 'W2', 'b2', 'W3', 'b3', 'Wo', 'bo')}
    del _L0_rec_all
    return {'r_sparse_embed': r_sparse_embed, 'L0_rec_W1': _L0_rec_in['W1'], 'L0_rec_b1': _L0_rec_in['b1'], 'L0_rec_W2': _L0_rec_in['W2'], 'L0_rec_b2': _L0_rec_in['b2'], 'L0_rec_W3': _L0_rec_in['W3'], 'L0_rec_b3': _L0_rec_in['b3'], 'L0_rec_Wo': _L0_rec_in['Wo'], 'L0_rec_bo': _L0_rec_in['bo']}

def reference(r_sparse_embed, L0_rec_W1, L0_rec_b1, L0_rec_W2, L0_rec_b2, L0_rec_W3, L0_rec_b3, L0_rec_Wo, L0_rec_bo):
    import jax
    import jax.numpy as jnp

    def _L0_rec_ref(sparse_embed, W1, b1, W2, b2, W3, b3, Wo, bo):
        import jax, jax.numpy as jnp
        import numpy as np
        NUM_FIELD = 32
        EMBED_DIM = 16
        BATCH = 256

        def _cin(x0, conv_params, split_flags):
            B, _, D = x0.shape
            x = x0
            results = []
            for (W, b), split in zip(conv_params, split_flags):
                h = x.shape[1]
                z = jnp.einsum('bhd,bmd->bhmd', x, x0).reshape(B, h * x0.shape[1], D)
                xk = jax.nn.relu(jnp.einsum('oc,bcd->bod', W, z) + b[None, :, None])
                if split:
                    half = xk.shape[1] // 2
                    x, xk = (xk[:, :half], xk[:, half:])
                else:
                    x = xk
                results.append(xk)
            return jnp.sum(jnp.concatenate(results, axis=1), axis=2)
        pooled = _cin(sparse_embed, [(W1, b1), (W2, b2), (W3, b3)], [True, True, False])
        return pooled @ Wo.T + bo
    y = _L0_rec_ref(r_sparse_embed, L0_rec_W1, L0_rec_b1, L0_rec_W2, L0_rec_b2, L0_rec_W3, L0_rec_b3, L0_rec_Wo, L0_rec_bo)
    return y

_drawn_inputs = setup_inputs


def setup_inputs(seed=0):
    import zlib

    import numpy as np

    out = dict(_drawn_inputs(seed))
    spreads = {'L0_rec_b1': (0.0, 0.1), 'L0_rec_b2': (0.0, 0.1), 'L0_rec_b3': (0.0, 0.1)}
    factors = {}
    for name, (base, spread) in spreads.items():
        noise = np.random.default_rng([zlib.crc32(name.encode()), seed]).standard_normal(out[name].shape)
        drawn = base * np.exp(spread * noise) if base else spread * noise
        out[name] = jnp.asarray(drawn.astype(out[name].dtype))
    for name, factor in factors.items():
        out[name] = (out[name] * factor).astype(out[name].dtype)
    return out
```

```python
from contextlib import ExitStack

import concourse.bass as bass
from concourse import mybir

F32 = mybir.dt.float32
F32R = mybir.dt.float32r
ALU = mybir.AluOpType
ACT = mybir.ActivationFunctionType
AX_X = mybir.AxisListType.X

P = 128
Q = 32
D = 16
BATCH = 512
N = BATCH * D
CH = 512
NCHUNK = N // CH
SAMPLES = CH // D
HALF = 64
GT = 2
RING = 6
SPLIT = {1: (1, 1), 2: (1, 1, 1, 2, 1, 1, 1, 2), 3: (1, 1, 1, 2, 1, 1, 1, 2)}
GROUPS = {layer: len(s) for layer, s in SPLIT.items()}
PER_ITER = sum(GROUPS.values())
FIRST = {1: 0, 2: GROUPS[1], 3: GROUPS[1] + GROUPS[2]}
BSLOTS = 3
LOOP = (4, NCHUNK - 1)


def tile_places(layer):
    native = [(g, t) for g, s in enumerate(SPLIT[layer]) for t in range(GT - s)]
    split = [(g, t) for g, s in enumerate(SPLIT[layer]) for t in range(GT - s, GT)]
    return native, split


def layers_of(i):
    return [layer for layer in (1, 2, 3) if 0 <= i - layer + 1 < NCHUNK]


def groups_before(i):
    if isinstance(i, int) and (i < 2 or i > NCHUNK):
        return sum(GROUPS[layer] for k in range(i) for layer in layers_of(k))
    return i * PER_ITER + (sum(GROUPS[layer] for k in range(2) for layer in layers_of(k)) - 2 * PER_ITER)


def groups_through(layer, c):
    i = c + layer - 1
    if isinstance(i, int):
        return groups_before(i) + sum(GROUPS[k] for k in layers_of(i) if k <= layer)
    return groups_before(i) + FIRST[layer] + GROUPS[layer]


def exists(chunk):
    return not isinstance(chunk, int) or 0 <= chunk < NCHUNK


def steps(i):
    found, q = [], groups_before(i)
    for layer in (1, 2, 3):
        if exists(i - (layer - 1)):
            for g in range(GROUPS[layer]):
                found.append((FIRST[layer] + g, layer, g, q + len(found)))
    return found


def slot_of(i, k):
    return (groups_before(i) + k) % RING if isinstance(i, int) else k % RING


assert groups_before(2) % RING == 0 and PER_ITER % RING == 0


def iterate(engine, body, last):
    for i in range(LOOP[0]):
        body(i)
    with engine.Fori(LOOP[0], LOOP[1]) as i:
        body(i)
    for i in range(LOOP[1], last + 1):
        body(i)


def cin_kernel(nc, xt, w1a, w1b, w1e, w2, w3, cols, bo, out):
    with ExitStack() as ctx:
        def sb(name, shape, dt=F32):
            return ctx.enter_context(nc.sbuf_tensor(name, shape, dt))

        def sem(name):
            return ctx.enter_context(nc.semaphore(name))

        nat = {layer: len(tile_places(layer)[0]) for layer in (1, 2, 3)}
        spl = {layer: len(tile_places(layer)[1]) for layer in (1, 2, 3)}

        w1_one = sb("w1_one", [P, 2 * GROUPS[1], P])
        w1_two = sb("w1_two", [P, 2 * GROUPS[1], P])
        w_raw = {1: sb("w1_sum", [P, 2 * GROUPS[1], P]), 2: sb("w2_raw", [P, 2 * GROUPS[2], P]),
                 3: sb("w3_raw", [P, 2 * GROUPS[3], P])}
        wh = {layer: sb(f"w{layer}_high", [P, spl[layer], P], F32R) for layer in (1, 2, 3)}
        wl = {layer: sb(f"w{layer}_low", [P, spl[layer], P], F32R) for layer in (1, 2, 3)}
        we_raw = sb("we_raw", [P, P])
        we = sb("we", [P, P], F32R)
        we_high = sb("we_high", [P, P], F32R)
        cols_sb = sb("cols_sb", [P, 5])
        bo_sb = sb("bo_sb", [1, 1])

        x_rep = sb("x_rep", [P, CH])
        shifted = sb("shifted", [P, 2 * GROUPS[1], CH])
        shifted_e = sb("shifted_e", [P, CH])
        b_fac = sb("b_fac", [P, BSLOTS * 8 * CH])
        z = sb("z", [P, RING, GT, CH])
        zh = sb("zh", [P, RING, GT, CH], F32R)
        zl = sb("zl", [P, RING, GT, CH], F32R)
        ze = sb("ze", [P, CH])
        ze_parts = sb("ze_parts", [P, CH], F32R)
        y_sb = {layer: sb(f"y{layer}_sb", [P, CH]) for layer in (1, 2, 3)}
        a_rep = {2: sb("a2_rep", [P, 2, CH]), 3: sb("a3_rep", [P, 2, CH])}
        pooled12 = sb("pooled12", [P, BATCH])
        pooled3 = sb("pooled3", [P, BATCH])
        out_sb = sb("out_sb", [1, BATCH])

        def psum(name, shape):
            return ctx.enter_context(nc.psum_tensor(name, shape, F32))

        x_ps = psum("x_ps", [P, CH])
        a_ps = {2: psum("a2_ps", [P, 2, CH]), 3: psum("a3_ps", [P, 2, CH])}
        y_ps = {layer: psum(f"y{layer}_ps", [P, CH]) for layer in (1, 2, 3)}

        w1_loaded = sem("w1_loaded")
        w23_loaded = {2: sem("w2_loaded"), 3: sem("w3_loaded")}
        cols_loaded = sem("cols_loaded")
        bo_loaded = sem("bo_loaded")
        zeroed = sem("zeroed")
        w1_summed = sem("w1_summed")
        w_rounded = {layer: sem(f"w{layer}_rounded") for layer in (1, 2, 3)}
        w_split = {layer: sem(f"w{layer}_split") for layer in (1, 2, 3)}
        we_rounded = sem("we_rounded")
        we_made = sem("we_made")
        x_loaded = sem("x_loaded")
        b_loaded = sem("b_loaded")
        x_in_psum = sem("x_in_psum")
        a_spread = {2: sem("a2_spread"), 3: sem("a3_spread")}
        a_in_psum = {2: sem("a2_in_psum"), 3: sem("a3_in_psum")}
        z_ready = sem("z_ready")
        zh_ready = sem("zh_ready")
        zl_ready = sem("zl_ready")
        group_used = sem("group_used")
        ze_ready = sem("ze_ready")
        ze_high_ready = sem("ze_high_ready")
        ze_low_ready = sem("ze_low_ready")
        y1_done = sem("y1_done")
        y_out = {layer: sem(f"y{layer}_out") for layer in (1, 2, 3)}
        pooled = {layer: sem(f"pooled{layer}_done") for layer in (1, 2, 3)}
        out_summed = sem("out_summed")
        out_ready = sem("out_ready")
        out_stored = sem("out_stored")
        X_DMAS, B_DMAS = 6, 4

        block = ctx.enter_context(nc.Block())

        @block.sync
        def _(sp):
            def load_x(c):
                if not isinstance(c, int) or c > 0:
                    sp.wait_ge(ze_ready, c)
                    sp.wait_ge(x_in_psum, c)
                n = bass.ds(c * CH, CH)
                sp.dma_start(x_rep[:], xt[0:Q, n].partition_broadcast(P // Q)).then_inc(x_loaded, 16)
                for s in range(4):
                    sp.dma_start(shifted[Q * s:Q * s + Q],
                                 xt_shift(s)[:, :, n]).then_inc(x_loaded, 16)
                sp.dma_start(shifted_e[:], xt[Q // 2:Q // 2 + Q, n].partition_broadcast(P // Q)
                             ).then_inc(x_loaded, 16)

            def xt_shift(s):
                return bass.AP(xt.tensor, s * N, [[N, Q], [4 * N, 4], [1, N]])

            def load_b(c):
                if not isinstance(c, int) or c > 0:
                    sp.wait_ge(b_loaded, c * (16 * B_DMAS))
                if not isinstance(c, int) or c >= BSLOTS:
                    sp.wait_ge(z_ready, groups_before(c))
                dst = b_fac[:, bass.ds((c % BSLOTS) * (8 * CH), 8 * CH)].rearrange("p (j n) -> p j n", j=8)
                for m in range(4):
                    src = bass.AP(xt.tensor, m * N, [[0, Q], [4 * N, 8], [1, N]])
                    sp.dma_start(dst[Q * m:Q * m + Q], src[:, :, bass.ds(c * CH, CH)]).then_inc(b_loaded, 16)

            def spread(layer, c):
                sp.wait_ge(y_out[layer], c + 1)
                top = {1: 0, 2: HALF}[layer]
                for k in range(2):
                    src = y_sb[layer][top + Q * k:top + Q * k + Q, :]
                    for quad in range(4):
                        sp.dma_start(a_rep[layer + 1][Q * quad:Q * quad + Q, k, :], src
                                     ).then_inc(a_spread[layer + 1], 16)

            sp.dma_start(cols_sb[:], cols).then_inc(cols_loaded, 16)
            sp.dma_start(w1_one[:], w1a).then_inc(w1_loaded, 16)
            sp.dma_start(w1_two[Q:P], w1b[Q:P]).then_inc(w1_loaded, 16)
            sp.dma_start(w1_two[0:Q, 1:], w1b[0:Q, 1:]).then_inc(w1_loaded, 16)
            sp.dma_start(we_raw[0:3 * Q], w1e).then_inc(w1_loaded, 16)
            load_x(0)
            sp.dma_start(w_raw[2][:], w2).then_inc(w23_loaded[2], 16)
            load_b(0)
            sp.dma_start(w_raw[3][:], w3).then_inc(w23_loaded[3], 16)
            sp.dma_start(bo_sb[:], bo).then_inc(bo_loaded, 16)

            def body(i):
                if exists(i + 1):
                    load_x(i + 1)
                if exists(i):
                    spread(1, i)
                if exists(i - 1):
                    spread(2, i - 1)
                if exists(i + 1):
                    load_b(i + 1)

            iterate(sp, body, NCHUNK)
            sp.wait_ge(out_ready, 1)
            sp.dma_start(out.rearrange("b o -> o b"), out_sb[:]).then_inc(out_stored, 16)
            sp.wait_ge(out_stored, 16)

        @block.scalar
        def _(act):
            def x_to_psum(c):
                act.wait_ge(x_loaded, (c + 1) * (16 * X_DMAS))
                if not isinstance(c, int) or c > 0:
                    act.wait_ge(ze_ready, c)
                nc.scalar.activation(x_ps[:], x_rep[:], ACT.Copy).then_inc(x_in_psum, 1)

            def a_to_psum(layer, c):
                act.wait_ge(a_spread[layer], (c + 1) * 128)
                nc.scalar.activation(a_ps[layer][:], a_rep[layer][:], ACT.Copy).then_inc(a_in_psum[layer], 1)

            def y_to_sbuf(layer, c):
                if layer == 1:
                    act.wait_ge(y1_done, c + 1)
                else:
                    act.wait_ge(group_used, groups_through(layer, c))
                if not isinstance(c, int) or c > 0:
                    act.wait_ge(pooled[layer], c)
                nc.scalar.activation(y_sb[layer][:], y_ps[layer][:], ACT.Relu,
                                     bias=cols_sb[:, layer - 1:layer]).then_inc(y_out[layer], 1)

            def round_w(layer):
                nc.scalar.activation(wh[layer][:], w_raw[layer][:, nat[layer]:, :], ACT.Copy
                                     ).then_inc(w_rounded[layer], 1)

            act.wait_ge(cols_loaded, 16)
            act.wait_ge(w1_loaded, 64)
            act.wait_ge(zeroed, 2)
            nc.scalar.activation(we_high[:], we_raw[:], ACT.Copy).then_inc(we_rounded, 1)
            nc.scalar.activation(we[:], we_raw[:], ACT.Copy).then_inc(we_rounded, 1)
            act.wait_ge(w1_summed, 1)
            round_w(1)
            x_to_psum(0)
            for layer in (2, 3):
                act.wait_ge(w23_loaded[layer], 16)
                round_w(layer)

            def body(i):
                here = {pos: (layer, g, q, k) for k, (pos, layer, g, q) in enumerate(steps(i))}
                for pos in range(PER_ITER):
                    if pos in here:
                        layer, g, q, k = here[pos]
                        s, slot = SPLIT[layer][g], slot_of(i, k)
                        act.wait_ge(z_ready, q + 1)
                        nc.scalar.activation(zh[:, slot, 0:s, :], z[:, slot, GT - s:, :], ACT.Copy
                                             ).then_inc(zh_ready, 1)
                    if pos == 1 and exists(i):
                        act.wait_ge(ze_ready, i + 1)
                        nc.scalar.activation(ze_parts[:], ze[:], ACT.Copy).then_inc(ze_high_ready, 1)
                    if pos == 3 and exists(i - 2):
                        a_to_psum(3, i - 2)
                    if pos == 6 and exists(i - 3):
                        y_to_sbuf(3, i - 3)
                    if pos == 8 and exists(i):
                        y_to_sbuf(1, i)
                    if pos == 10 and exists(i + 1):
                        x_to_psum(i + 1)
                    if pos == 13 and exists(i):
                        a_to_psum(2, i)
                    if pos == 15 and exists(i - 1):
                        y_to_sbuf(2, i - 1)

            iterate(act, body, NCHUNK + 2)

        @block.gpsimd
        def _(pool):
            nc.gpsimd.memset(w1_two[0:Q, 0:1, :], 0.0).then_inc(zeroed, 1)
            nc.gpsimd.memset(we_raw[3 * Q:P, :], 0.0).then_inc(zeroed, 1)

            def body(i):
                for k, (pos, layer, g, q) in enumerate(steps(i)):
                    s, slot = SPLIT[layer][g], slot_of(i, k)
                    pool.wait_ge(zh_ready, q + 1)
                    nc.gpsimd.tensor_tensor(zl[:, slot, 0:s, :], z[:, slot, GT - s:, :],
                                            zh[:, slot, 0:s, :].bitcast(F32), ALU.subtract
                                            ).then_inc(zl_ready, 1)

            iterate(pool, body, NCHUNK + 1)

        @block.vector
        def _(dve):
            def split_w(layer):
                nc.vector.tensor_tensor(wl[layer][:], w_raw[layer][:, nat[layer]:, :],
                                        wh[layer][:].bitcast(F32), ALU.subtract).then_inc(w_split[layer], 1)

            def pool_dims(layer, c):
                dve.wait_ge(y_out[layer], c + 1)
                rows = {1: slice(HALF, P), 2: slice(0, HALF), 3: slice(0, P)}[layer]
                dst = pooled3 if layer == 3 else pooled12
                nc.vector.tensor_reduce(dst[rows, bass.ds(c * SAMPLES, SAMPLES)],
                                        y_sb[layer][rows, :].rearrange("p (b d) -> p b d", d=D),
                                        AX_X, ALU.add).then_inc(pooled[layer], 1)

            dve.wait_ge(w1_loaded, 64)
            dve.wait_ge(zeroed, 2)
            nc.vector.tensor_tensor(w_raw[1][:], w1_one[:], w1_two[:], ALU.add).then_inc(w1_summed, 1)
            dve.wait_ge(we_rounded, 2)
            nc.vector.tensor_tensor(we[2 * Q:3 * Q, :], we_raw[2 * Q:3 * Q, :],
                                    we_high[2 * Q:3 * Q, :].bitcast(F32), ALU.subtract).then_inc(we_made, 1)
            dve.wait_ge(w1_summed, 1)
            dve.wait_ge(w_rounded[1], 1)
            split_w(1)

            def split_e(c):
                dve.wait_ge(ze_high_ready, c + 1)
                low = ze_parts[Q:2 * Q, :]
                nc.vector.tensor_tensor(low, ze[Q:2 * Q, :], low.bitcast(F32), ALU.subtract
                                        ).then_inc(ze_low_ready, 1)

            def body(i):
                if exists(i):
                    dve.wait_ge(x_loaded, (i + 1) * (16 * X_DMAS))
                    dve.wait_ge(x_in_psum, i + 1)
                if isinstance(i, int) and i in (1, 2):
                    dve.wait_ge(w_rounded[i + 1], 1)
                    split_w(i + 1)
                for k, (pos, layer, g, q) in enumerate(steps(i)):
                    c, slot = i - (layer - 1), slot_of(i, k)
                    if g == 0 and layer > 1:
                        dve.wait_ge(a_in_psum[layer], c + 1)
                    if g == 0 and layer == 2:
                        dve.wait_ge(b_loaded, (c + 1) * (16 * B_DMAS))
                    if not isinstance(q, int) or q >= RING:
                        dve.wait_ge(group_used, q - (RING - 1))
                    if layer == 1:
                        other = shifted[:, GT * g:GT * g + GT, :]
                        rep = x_ps[:]
                    else:
                        half, j = divmod(g, GROUPS[layer] // 2)
                        other = b_fac[:, bass.ds((c % BSLOTS) * (8 * CH) + GT * j * CH, GT * CH)
                                      ].rearrange("p (j n) -> p j n", j=GT)
                        rep = a_ps[layer][:, half, :]
                    nc.vector.tensor_tensor(z[:, slot, :, :], rep.unsqueeze(1).to_broadcast([P, GT, CH]),
                                            other, ALU.mult).then_inc(z_ready, 1)
                    if layer == 1 and g == GROUPS[1] - 1:
                        if not isinstance(i, int) or i > 0:
                            dve.wait_ge(ze_low_ready, i)
                        nc.vector.tensor_tensor(ze[:], x_ps[:], shifted_e[:], ALU.mult).then_inc(ze_ready, 1)
                    if pos == 2 and exists(i):
                        split_e(i)
                    if pos == 2 and exists(i - 2):
                        pool_dims(2, i - 2)
                    if pos == 10 and exists(i - 3):
                        pool_dims(3, i - 3)
                    if pos == 14 and exists(i):
                        pool_dims(1, i)
                if isinstance(i, int):
                    there = {s[0] for s in steps(i)}
                    if 2 not in there and exists(i):
                        split_e(i)
                    for pos, layer, c in ((2, 2, i - 2), (10, 3, i - 3), (14, 1, i)):
                        if pos not in there and exists(c):
                            pool_dims(layer, c)

            iterate(dve, body, NCHUNK + 2)
            dve.wait_ge(out_summed, 1)
            dve.wait_ge(bo_loaded, 16)
            nc.vector.tensor_scalar(out_sb[:], y_ps[1][0:1, :], bo_sb[0:1, 0:1], None, ALU.add
                                    ).then_inc(out_ready, 1)

        @block.tensor
        def _(pe):
            def body(i):
                for k, (pos, layer, g, q) in enumerate(steps(i)):
                    c, slot, s = i - (layer - 1), slot_of(i, k), SPLIT[layer][g]
                    native, split = tile_places(layer)
                    y = y_ps[layer][:]
                    if g == 0 and (not isinstance(c, int) or c > 0):
                        pe.wait_ge(y_out[layer], c)
                    if isinstance(i, int) and g == 0 and i == layer - 1:
                        pe.wait_ge(w_split[layer], 1)
                    last = layer > 1 and g == GROUPS[layer] - 1
                    pe.wait_ge(z_ready, q + 1)
                    for t in range(GT - s):
                        nc.tensor.matmul(y, w_raw[layer][:, native.index((g, t)), :], z[:, slot, t, :],
                                         start=(g == 0 and t == 0), stop=False)
                    pe.wait_ge(zh_ready, q + 1)
                    places = [(t, split.index((g, GT - s + t))) for t in range(s)]
                    for t, w in places:
                        nc.tensor.matmul(y, wh[layer][:, w, :], zh[:, slot, t, :],
                                         start=(g == 0 and s == GT and t == 0), stop=False)
                        nc.tensor.matmul(y, wl[layer][:, w, :], zh[:, slot, t, :], start=False, stop=False)
                    pe.wait_ge(zl_ready, q + 1)
                    for t, w in places:
                        mm = nc.tensor.matmul(y, wh[layer][:, w, :], zl[:, slot, t, :],
                                              start=False, stop=(last and t == s - 1))
                    mm.then_inc(group_used, 1)
                    if layer == 1 and g == GROUPS[1] - 1:
                        if isinstance(i, int) and i == 0:
                            pe.wait_ge(we_made, 1)
                        pe.wait_ge(ze_low_ready, i + 1)
                        nc.tensor.matmul(y, we[:], ze_parts[:], start=False, stop=True).then_inc(y1_done, 1)

            iterate(pe, body, NCHUNK + 1)

            for layer in (1, 2, 3):
                pe.wait_ge(pooled[layer], NCHUNK)
            nc.tensor.matmul(y_ps[1][0:1, :], cols_sb[:, 3:4], pooled12[:], start=True, stop=False)
            nc.tensor.matmul(y_ps[1][0:1, :], cols_sb[:, 4:5], pooled3[:], start=False, stop=True
                             ).then_inc(out_summed, 1)


def tiles_on_host(w, layer):
    native, split = tile_places(layer)
    return w[:, [g * GT + t for g, t in native + split], :]


def kernel(r_sparse_embed, L0_rec_W1, L0_rec_b1, L0_rec_W2, L0_rec_b2, L0_rec_W3, L0_rec_b3,
           L0_rec_Wo, L0_rec_bo):
    import numpy as np
    import concourse.bacc as bacc
    from concourse.bass_utils import run_bass_kernel_spmd as run

    x = np.asarray(r_sparse_embed).transpose(1, 0, 2).reshape(Q, N)
    roll = np.r_[HALF:P, 0:HALF]
    W1 = np.asarray(L0_rec_W1).reshape(P, Q, Q)
    h = np.arange(Q)[None, :, None]
    shift = (4 * np.arange(4)[None, None, :] + np.arange(4)[:, None, None])
    w1a = W1[:, h, (h + shift) % Q].transpose(1, 2, 3, 0).reshape(P, 4, P)
    w1b = W1[:, (h + shift) % Q, h].transpose(1, 2, 3, 0).reshape(P, 4, P)
    k = np.arange(Q)
    w1e = np.tile(W1[:, k, (k + Q // 2) % Q].T, (3, 1))

    def blocks(W, layer):
        w = np.asarray(W).reshape(P, 2, Q, 8, 4).transpose(4, 2, 1, 3, 0).reshape(P, 16, P)
        return tiles_on_host(w, layer)

    Wo = np.asarray(L0_rec_Wo)[0]
    arrays = {
        "xt": np.concatenate([x, x[:Q // 2]]),
        "w1a": tiles_on_host(w1a, 1), "w1b": tiles_on_host(w1b, 1), "w1e": w1e,
        "w2": blocks(np.asarray(L0_rec_W2)[roll], 2), "w3": blocks(L0_rec_W3, 3),
        "cols": np.stack([np.asarray(L0_rec_b1), np.asarray(L0_rec_b2)[roll], np.asarray(L0_rec_b3),
                          Wo[:P][roll], Wo[P:]], axis=1),
        "bo": np.asarray(L0_rec_bo).reshape(1, 1),
    }
    arrays = {f"{n}_dram": np.ascontiguousarray(a) for n, a in arrays.items()}
    nc = bacc.Bacc("TRN2", target_bir_lowering=False, num_devices=1)
    args = [nc.dram_tensor(n, a.shape, F32, kind="ExternalInput").ap() for n, a in arrays.items()]
    args.append(nc.dram_tensor("out_dram", (BATCH, 1), F32, kind="ExternalOutput").ap())
    cin_kernel(nc, *args)
    return run(nc, [arrays], core_ids=[0]).results[0]["out_dram"]
```

```python
from contextlib import ExitStack

import concourse.bass as bass
from concourse import mybir

F32 = mybir.dt.float32
F32R = mybir.dt.float32r
ALU = mybir.AluOpType
ACT = mybir.ActivationFunctionType
AX_X = mybir.AxisListType.X

P = 128
Q = 32
D = 16
BATCH = 512
N = BATCH * D
CH = 512
NCHUNK = N // CH
SAMPLES = CH // D
HALF = 64
GT = 4
RING = 3
SPLIT = {1: (2,), 2: (3, 3, 3, 3), 3: (3, 3, 3, 3)}
BY_DVE = {1: (1,), 2: (1, 0, 1, 0), 3: (1, 0, 1, 0)}
ZX_BANK = {0: 1, 1: 0, 3: 1, 5: 0, 7: 1}
QUARTER = {1: 1, 2: 0, 3: 0}
PARTS = 3
ZT = 4
GROUPS = {layer: len(s) for layer, s in SPLIT.items()}
PER_ITER = sum(GROUPS.values())
DVE_PER_ITER = sum(n for by_dve in BY_DVE.values() for n in by_dve)
FIRST = {1: 0, 2: GROUPS[1], 3: GROUPS[1] + GROUPS[2]}
BSLOTS = 3
XSLOTS = 2
NAT1 = GT - SPLIT[1][0]
XT = GT + 1
XQ = GT - BY_DVE[1][0]
LOOP = (4, NCHUNK - 2)


def tile_places(layer):
    native = [(g, t) for g, s in enumerate(SPLIT[layer]) for t in range(GT - s)]
    split = [(g, t) for g, s in enumerate(SPLIT[layer]) for t in range(GT - s, GT)]
    return native, split


def layers_of(i):
    return [layer for layer in (1, 2, 3) if 0 <= i - layer + 1 < NCHUNK]


def groups_before(i):
    if isinstance(i, int) and (i < 2 or i > NCHUNK):
        return sum(GROUPS[layer] for k in range(i) for layer in layers_of(k))
    return i * PER_ITER + (sum(GROUPS[layer] for k in range(2) for layer in layers_of(k)) - 2 * PER_ITER)


def dve_tiles_before(i):
    if isinstance(i, int) and (i < 2 or i > NCHUNK):
        return sum(sum(BY_DVE[layer]) for k in range(1, i) for layer in layers_of(k))
    return i * DVE_PER_ITER + (sum(BY_DVE[1] + BY_DVE[2]) - 2 * DVE_PER_ITER)


def groups_through(layer, c):
    i = c + layer - 1
    if isinstance(i, int):
        return groups_before(i) + sum(GROUPS[k] for k in layers_of(i) if k <= layer)
    return groups_before(i) + FIRST[layer] + GROUPS[layer]


def i_is(i, number):
    return isinstance(i, int) and i == number


def exists(chunk):
    return not isinstance(chunk, int) or 0 <= chunk < NCHUNK


def steps(i):
    found, q, e = [], groups_before(i), dve_tiles_before(i)
    for layer in (1, 2, 3):
        if exists(i - (layer - 1)):
            for g in range(GROUPS[layer]):
                found.append((FIRST[layer] + g, layer, g, q + len(found), e))
                e = e + BY_DVE[layer][g]
    return found


def parts_of(layer, g):
    by_dve = BY_DVE[layer][g]
    return GT - SPLIT[layer][g], GT + QUARTER[layer] - by_dve, by_dve


def slot_of(i, k):
    return (groups_before(i) + k) % RING if isinstance(i, int) else k % RING


assert groups_before(2) % RING == 0 and PER_ITER % RING == 0


def iterate(engine, body, last):
    for i in range(LOOP[0]):
        body(i)
    with engine.Fori(LOOP[0], LOOP[1]) as i:
        body(i)
    for i in range(LOOP[1], last + 1):
        body(i)


def cin_kernel(nc, xt, w1, w2, w3, cols, bo, out):
    with ExitStack() as ctx:
        def sb(name, shape, dt=F32):
            return ctx.enter_context(nc.sbuf_tensor(name, shape, dt))

        def sem(name):
            return ctx.enter_context(nc.semaphore(name))

        nat = {layer: len(tile_places(layer)[0]) for layer in (1, 2, 3)}
        spl = {layer: len(tile_places(layer)[1]) for layer in (1, 2, 3)}

        w1_sb = sb("w1_sb", [P, 2 * GT + 2, P])
        w_raw = {1: sb("w1_sum", [P, GT * GROUPS[1], P]), 2: sb("w2_raw", [P, GT * GROUPS[2], P]),
                 3: sb("w3_raw", [P, GT * GROUPS[3], P])}
        wh = {layer: sb(f"w{layer}_high", [P, spl[layer], P], F32R) for layer in (1, 2, 3)}
        wl = {layer: sb(f"w{layer}_low", [P, spl[layer], P], F32R) for layer in (1, 2, 3)}
        wq_raw = w1_sb[:, 2 * GT:, :]
        wq = sb("wq", [P, 2, P], F32R)
        cols_sb = sb("cols_sb", [P, 5])
        bo_sb = sb("bo_sb", [1, 1])

        x_rep = sb("x_rep", [P, XSLOTS * CH])
        shifted = sb("shifted", [P, XSLOTS * XT * CH])
        b_fac = sb("b_fac", [P, BSLOTS * 8 * CH])
        z = sb("z", [P, RING, ZT, CH])
        zh = sb("zh", [P, RING, PARTS, CH], F32R)
        zl = sb("zl", [P, RING, PARTS, CH], F32R)
        y_sb = {layer: sb(f"y{layer}_sb", [P, CH]) for layer in (1, 2, 3)}
        a_rep = {2: sb("a2_rep", [P, 2, CH]), 3: sb("a3_rep", [P, 2, CH])}
        pooled12 = sb("pooled12", [P, BATCH])
        pooled3 = sb("pooled3", [P, BATCH])
        out_sb = sb("out_sb", [1, BATCH])

        def psum(name, shape):
            return ctx.enter_context(nc.psum_tensor(name, shape, F32))

        x_ps = psum("x_ps", [P, CH])
        a_ps = psum("a_ps", [P, 2, CH])
        zx_ps = psum("zx_ps", [P, 2, CH])
        y_ps = {layer: psum(f"y{layer}_ps", [P, CH]) for layer in (1, 2, 3)}

        w1_loaded = sem("w1_loaded")
        w1_rest_loaded = sem("w1_rest_loaded")
        w23_loaded = {2: sem("w2_loaded"), 3: sem("w3_loaded")}
        cols_loaded = sem("cols_loaded")
        bo_loaded = sem("bo_loaded")
        w1_summed = sem("w1_summed")
        w1_rest_summed = sem("w1_rest_summed")
        w_rounded = {layer: sem(f"w{layer}_rounded") for layer in (1, 2, 3)}
        w_split = {layer: sem(f"w{layer}_split") for layer in (1, 2, 3)}
        wq_rounded = sem("wq_rounded")
        wq_made = sem("wq_made")
        x0_loaded = (sem("x0_native_loaded"), sem("x0_rest_loaded"))
        x_loaded = (sem("x_native_loaded"), sem("x_rest_loaded"))
        b0_loaded = (sem("b0_loaded"), sem("b0_rest_loaded"))
        b_loaded = sem("b_loaded")
        x_in_psum = sem("x_in_psum")
        a_spread = {2: (sem("a2_0_spread"), sem("a2_1_spread")),
                    3: (sem("a3_0_spread"), sem("a3_1_spread"))}
        a_in_psum = {2: (sem("a2_0_in_psum"), sem("a2_1_in_psum")),
                     3: (sem("a3_0_in_psum"), sem("a3_1_in_psum"))}
        z_native_ready = sem("z_native_ready")
        z_ready = sem("z_ready")
        zh_ready = sem("zh_ready")
        zl_ready = sem("zl_ready")
        zx_ready = sem("zx_ready")
        zxh_ready = sem("zxh_ready")
        zxl_ready = sem("zxl_ready")
        zx0_ready = sem("zx0_ready")
        group_used = sem("group_used")
        y_out = {layer: sem(f"y{layer}_out") for layer in (1, 2, 3)}
        pooled = {layer: sem(f"pooled{layer}_done") for layer in (1, 2, 3)}
        out_summed = sem("out_summed")
        out_ready = sem("out_ready")
        out_stored = sem("out_stored")
        X_DMAS, B_DMAS, A_DMAS = 3, 4, (2, 3)

        def bank(layer, c):
            return y_ps[2] if layer == 3 and i_is(c, NCHUNK - 1) else y_ps[layer]

        block = ctx.enter_context(nc.Block())

        @block.sync
        def _(sp):
            def load_x(c, parts=(0, 1)):
                if not isinstance(c, int) or c > 1:
                    for part in parts:
                        sp.wait_ge(x_loaded[part], (c - 1) * (16 * X_DMAS))
                if not isinstance(c, int) or c >= XSLOTS:
                    sp.wait_ge(z_ready, groups_through(1, c - XSLOTS))
                n = bass.ds(c * CH, CH)
                slot = c % XSLOTS
                loaded = x0_loaded if i_is(c, 0) else x_loaded
                if 0 in parts:
                    sp.dma_start(x_rep[:, bass.ds(slot * CH, CH)], xt[0:Q, n].partition_broadcast(P // Q)
                                 ).then_inc(loaded[0], 16)
                for t in range(GT):
                    part = 0 if t < NAT1 else 1
                    if part in parts:
                        src = bass.AP(xt.tensor, 4 * t * N, [[N, 4], [N, Q], [1, N]])
                        place = t if t < XQ else t + 1
                        sp.dma_start(shifted[:, bass.ds(slot * (XT * CH) + place * CH, CH)], src[:, :, n]
                                     ).then_inc(loaded[part], 16)
                if 1 in parts:
                    sp.dma_start(shifted[:, bass.ds(slot * (XT * CH) + XQ * CH, CH)],
                                 xt[Q // 2:Q // 2 + Q, n].partition_broadcast(P // Q)
                                 ).then_inc(loaded[1], 16)

            def load_b(c, parts=None):
                if not isinstance(c, int) or c > 1:
                    sp.wait_ge(b_loaded, (c - 1) * (16 * B_DMAS))
                if not isinstance(c, int) or c >= BSLOTS:
                    sp.wait_ge(z_ready, groups_before(c))
                for j, end, loaded in parts or ((0, 8, b_loaded),):
                    size = (end - j) * CH
                    dst = b_fac[:, bass.ds((c % BSLOTS) * (8 * CH) + j * CH, size)
                                ].rearrange("p (j n) -> p j n", j=end - j)
                    for m in range(4):
                        src = bass.AP(xt.tensor, (4 * j + m) * N, [[0, Q], [4 * N, end - j], [1, N]])
                        sp.dma_start(dst[Q * m:Q * m + Q], src[:, :, bass.ds(c * CH, CH)]).then_inc(loaded, 16)

            def spread(layer, c):
                sp.wait_ge(y_out[layer], c + 1)
                top = {1: 0, 2: HALF}[layer]
                for k, to, rows, count in ((0, 0, 0, 2), (0, 2, 0, 2), (1, 1, 0, 2), (1, 3, 0, 1), (1, 0, 1, 1)):
                    sp.dma_start(a_rep[layer + 1][Q * to:Q * (to + count), k, :],
                                 y_sb[layer][top + Q * rows:top + Q * (rows + count), :]
                                 ).then_inc(a_spread[layer + 1][k], 16)

            load_x(0, (0,))
            sp.dma_start(w1_sb[:, 0:2 * NAT1], w1[:, 0:2 * NAT1]).then_inc(w1_loaded, 16)
            load_x(0, (1,))
            sp.dma_start(w1_sb[:, 2 * NAT1:], w1[:, 2 * NAT1:]).then_inc(w1_rest_loaded, 16)
            sp.dma_start(cols_sb[:], cols).then_inc(cols_loaded, 16)
            load_x(1)
            sp.dma_start(w_raw[2][:], w2).then_inc(w23_loaded[2], 16)
            load_b(0, ((0, 4, b0_loaded[0]),))

            def body(i):
                if exists(i):
                    spread(1, i)
                if i_is(i, 0):
                    load_b(0, ((4, 8, b0_loaded[1]),))
                if exists(i + 2):
                    load_x(i + 2)
                if exists(i - 1):
                    spread(2, i - 1)
                if exists(i + 1):
                    load_b(i + 1)
                if i_is(i, 0):
                    sp.dma_start(w_raw[3][:], w3).then_inc(w23_loaded[3], 16)
                    sp.dma_start(bo_sb[:], bo).then_inc(bo_loaded, 16)

            iterate(sp, body, NCHUNK)
            sp.wait_ge(out_ready, 1)
            sp.dma_start(out.rearrange("b o -> o b"), out_sb[:]).then_inc(out_stored, 16)
            sp.wait_ge(out_stored, 16)

        @block.scalar
        def _(act):
            def x_to_psum(c):
                act.wait_ge(x_loaded[0], c * (16 * X_DMAS))
                nc.scalar.activation(x_ps[:], x_rep[:, bass.ds((c % XSLOTS) * CH, CH)], ACT.Copy).then_inc(x_in_psum, 1)

            def a_to_psum(layer, half, c):
                act.wait_ge(a_spread[layer][half], (c + 1) * (16 * A_DMAS[half]))
                nc.scalar.activation(a_ps[:, half, :], a_rep[layer][:, half, :], ACT.Copy
                                     ).then_inc(a_in_psum[layer][half], 1)

            def y_to_sbuf(layer, c):
                act.wait_ge(group_used, groups_through(layer, c))
                if not isinstance(c, int) or c > 0:
                    act.wait_ge(pooled[layer], c)
                if i_is(c, 0) and layer == 1:
                    act.wait_ge(cols_loaded, 16)
                nc.scalar.activation(y_sb[layer][:], bank(layer, c)[:], ACT.Relu,
                                     bias=cols_sb[:, layer - 1:layer]).then_inc(y_out[layer], 1)

            def round_w(layer):
                if layer > 1:
                    act.wait_ge(w23_loaded[layer], 16)
                nc.scalar.activation(wh[layer][:], w_raw[layer][:, nat[layer]:, :], ACT.Copy
                                     ).then_inc(w_rounded[layer], 1)

            act.wait_ge(w1_rest_summed, 1)
            nc.scalar.activation(wq[:], wq_raw, ACT.Copy).then_inc(wq_rounded, 1)
            round_w(1)

            def body(i):
                here = {step[0]: (step, k) for k, step in enumerate(steps(i))}
                for pos in range(PER_ITER):
                    if pos in here and not i_is(i, 0):
                        (pos, layer, g, q, e), k = here[pos]
                        slot, (native, end, by_dve) = slot_of(i, k), parts_of(layer, g)
                        act.wait_ge(z_ready, q + 1)
                        nc.scalar.activation(zh[:, slot, 0:end - native, :], z[:, slot, native:end, :], ACT.Copy
                                             ).then_inc(zh_ready, 1)
                        if by_dve:
                            act.wait_ge(zx_ready, e + 1)
                            nc.scalar.activation(zh[:, slot, end - native, :], zx_ps[:, ZX_BANK[pos], :], ACT.Copy
                                                 ).then_inc(zxh_ready, 1)
                    if pos == 0 and i_is(i, 0):
                        y_to_sbuf(1, 0)
                    if pos == 0 and i_is(i, 1):
                        round_w(2)
                        a_to_psum(2, 0, 0)
                    if pos == 1 and i_is(i, 1):
                        a_to_psum(2, 1, 0)
                    if pos == 0 and i_is(i, 2):
                        a_to_psum(2, 0, 1)
                        y_to_sbuf(2, 0)
                    if pos == 2 and i_is(i, 2):
                        round_w(3)
                    if pos == (1 if i_is(i, 2) else 0) and exists(i - 1) and not i_is(i, 1):
                        a_to_psum(2, 1, i - 1)
                    if pos == 3 and exists(i - 2):
                        a_to_psum(3, 0, i - 2)
                    if pos == 5 and exists(i - 2):
                        a_to_psum(3, 1, i - 2)
                    if pos == (6 if i_is(i, NCHUNK + 1) else 3) and exists(i - 3):
                        y_to_sbuf(3, i - 3)
                    if pos == 4 and exists(i) and not i_is(i, 0):
                        y_to_sbuf(1, i)
                    if pos == 5 and exists(i + 1) and not i_is(i, 0):
                        x_to_psum(i + 1)
                    if pos == 7 and exists(i) and not i_is(i, 0) and not i_is(i, 1):
                        a_to_psum(2, 0, i)
                    if pos == (6 if i_is(i, NCHUNK) else 7) and exists(i - 1) and not i_is(i, 1):
                        y_to_sbuf(2, i - 1)

            iterate(act, body, NCHUNK + 2)

        @block.gpsimd
        def _(pool):
            pool.wait_ge(w1_rest_loaded, 16)
            nc.gpsimd.tensor_tensor(w_raw[1][:, NAT1:, :], w1_sb[:, 2 * NAT1:GT + NAT1, :],
                                    w1_sb[:, GT + NAT1:2 * GT, :], ALU.add).then_inc(w1_rest_summed, 1)

            def body(i):
                if i_is(i, 0):
                    return
                for k, (pos, layer, g, q, e) in enumerate(steps(i)):
                    slot, (native, end, by_dve) = slot_of(i, k), parts_of(layer, g)
                    pool.wait_ge(zh_ready, q)
                    nc.gpsimd.tensor_tensor(zl[:, slot, 0:end - native, :], z[:, slot, native:end, :],
                                            zh[:, slot, 0:end - native, :].bitcast(F32), ALU.subtract
                                            ).then_inc(zl_ready, 1)

            iterate(pool, body, NCHUNK + 1)

        @block.vector
        def _(dve):
            def split_w(layer):
                nc.vector.tensor_tensor(wl[layer][:], w_raw[layer][:, nat[layer]:, :],
                                        wh[layer][:].bitcast(F32), ALU.subtract).then_inc(w_split[layer], 1)

            def pool_dims(layer, c):
                dve.wait_ge(y_out[layer], c + 1)
                rows = {1: slice(HALF, P), 2: slice(0, HALF), 3: slice(0, P)}[layer]
                dst = pooled3 if layer == 3 else pooled12
                nc.vector.tensor_reduce(dst[rows, bass.ds(c * SAMPLES, SAMPLES)],
                                        y_sb[layer][rows, :].rearrange("p (b d) -> p b d", d=D),
                                        AX_X, ALU.add).then_inc(pooled[layer], 1)


            def multiply(dst, factor, others):
                return nc.vector.tensor_tensor(dst, factor.unsqueeze(1).to_broadcast(list(dst.shape)), others, ALU.mult)

            def product(i, step, k):
                pos, layer, g, q, e = step
                c, slot, (native, end, by_dve) = i - (layer - 1), slot_of(i, k), parts_of(layer, g)
                if layer > 1:
                    half, j = divmod(g, GROUPS[layer] // 2)
                    if j == 0:
                        dve.wait_ge(a_in_psum[layer][half], c + 1)
                if layer == 2 and i_is(c, 0):
                    if half == 0:
                        dve.wait_ge(b0_loaded[j], 16 * B_DMAS)
                elif layer == 2 and g == 0:
                    dve.wait_ge(b_loaded, c * (16 * B_DMAS))
                if not isinstance(q, int) or q >= RING:
                    dve.wait_ge(group_used, q - (RING - 1))
                elif q == RING - 1:
                    dve.wait_ge(group_used, 1)
                start = 0
                if layer == 1:
                    others = shifted[:, bass.ds((c % XSLOTS) * (XT * CH), XT * CH)
                                     ].rearrange("p (t n) -> p t n", t=XT)
                    if i_is(c, 0) or i_is(c, 1):
                        factor = x_rep[:, c * CH:(c + 1) * CH]
                        dve.wait_ge((x0_loaded, x_loaded)[c][0], 16 * X_DMAS)
                    else:
                        factor = x_ps[:]
                        dve.wait_ge(x_in_psum, c - 1)
                    start = native
                    multiply(z[:, slot, 0:start, :], factor, others[:, 0:start, :]).then_inc(z_native_ready, 1)
                    if i_is(c, 0):
                        dve.wait_ge(w1_loaded, 16)
                        nc.vector.tensor_tensor(w_raw[1][:, 0:NAT1, :], w1_sb[:, 0:NAT1, :],
                                                w1_sb[:, NAT1:2 * NAT1, :], ALU.add).then_inc(w1_summed, 1)
                        dve.wait_ge(x0_loaded[1], 16 * X_DMAS)
                    else:
                        dve.wait_ge(x_loaded[1], c * (16 * X_DMAS))
                else:
                    others = b_fac[:, bass.ds((c % BSLOTS) * (8 * CH) + GT * j * CH, GT * CH)
                                   ].rearrange("p (j n) -> p j n", j=GT)
                    factor = a_ps[:, half, :]
                multiply(z[:, slot, start:end, :], factor, others[:, start:end, :]).then_inc(z_ready, 1)
                if by_dve and i_is(i, 0):
                    multiply(z[:, RING - 1, 0:1, :], factor, others[:, end:, :]).then_inc(zx0_ready, 1)
                elif by_dve:
                    done = e - 1 if pos == 1 else e
                    if not isinstance(e, int) or done > 0:
                        dve.wait_ge(zxl_ready, done)
                    bank = ZX_BANK[pos]
                    multiply(zx_ps[:, bank:bank + 1, :], factor, others[:, end:, :]).then_inc(zx_ready, 1)

            def subtract(i, step, k):
                pos, layer, g, q, e = step
                slot, (native, end, by_dve) = slot_of(i, k), parts_of(layer, g)
                dve.wait_ge(zxh_ready, e + 1)
                nc.vector.tensor_tensor(zl[:, slot, end - native, :], zx_ps[:, ZX_BANK[pos], :],
                                        zh[:, slot, end - native, :].bitcast(F32), ALU.subtract
                                        ).then_inc(zxl_ready, 1)

            def body(i):
                here = {s[0]: (s, k) for k, s in enumerate(steps(i))}
                for pos in range(PER_ITER):
                    if pos in here:
                        product(i, *here[pos])
                    if i_is(i, 1) and pos == 0:
                        subtract(i, *here[0])
                    elif pos - 1 in here and pos - 1 in ZX_BANK and not i_is(i, 0) and not (i_is(i, 1) and pos == 1):
                        subtract(i, *here[pos - 1])
                    if pos == 0 and i_is(i, 0):
                        dve.wait_ge(wq_rounded, 1)
                        nc.vector.tensor_tensor(wq[Q:2 * Q, 0, :], wq_raw[Q:2 * Q, 0, :],
                                                wq[Q:2 * Q, 0, :].bitcast(F32), ALU.subtract).then_inc(wq_made, 1)
                        dve.wait_ge(w_rounded[1], 1)
                        split_w(1)
                    if pos == 0 and i_is(i, 1):
                        dve.wait_ge(w_rounded[2], 1)
                        split_w(2)
                    if pos == 3 and i_is(i, 2):
                        dve.wait_ge(w_rounded[3], 1)
                        split_w(3)
                    if pos == 1 and (i_is(i, 1) or i_is(i, 2)):
                        pool_dims(1, i - 1)
                    if pos == (2 if i_is(i, 2) else 1) and exists(i - 2):
                        pool_dims(2, i - 2)
                    if pos == (7 if i_is(i, NCHUNK + 1) else 5) and exists(i - 3):
                        pool_dims(3, i - 3)
                    if pos == 7 and exists(i) and not i_is(i, 0) and not i_is(i, 1):
                        pool_dims(1, i)

            iterate(dve, body, NCHUNK + 2)
            dve.wait_ge(out_summed, 1)
            dve.wait_ge(bo_loaded, 16)
            nc.vector.tensor_scalar(out_sb[:], y_ps[1][0:1, :], bo_sb[0:1, 0:1], None, ALU.add
                                    ).then_inc(out_ready, 1)

        @block.tensor
        def _(pe):
            def dot(part, column, rows, start, stop):
                return nc.tensor.matmul(y_ps[1][0:1, rows], cols_sb[:, column:column + 1], part[:, rows],
                                        start=start, stop=stop)

            def body(i):
                for k, (pos, layer, g, q, e) in enumerate(steps(i)):
                    if i_is(i, NCHUNK + 1) and g == GROUPS[3] - 1:
                        for done in (1, 2):
                            pe.wait_ge(pooled[done], NCHUNK)
                        dot(pooled12, 3, slice(0, BATCH), True, False)
                        pe.wait_ge(pooled[3], NCHUNK - 1)
                        dot(pooled3, 4, slice(0, BATCH - SAMPLES), False, False)
                    c, slot, (native, end, by_dve) = i - (layer - 1), slot_of(i, k), parts_of(layer, g)
                    y = bank(layer, c)[:]
                    if g == 0 and layer == 3 and i_is(c, NCHUNK - 1):
                        pe.wait_ge(y_out[2], NCHUNK)
                    elif g == 0 and (not isinstance(c, int) or c > 0):
                        pe.wait_ge(y_out[layer], c)
                    if i_is(i, 0):
                        pe.wait_ge(w1_summed, 1)
                        pe.wait_ge(z_native_ready, 1)
                        for t in range(NAT1):
                            nc.tensor.matmul(y, w_raw[1][:, t, :], z[:, 0, t, :], start=(t == 0), stop=False)
                        pe.wait_ge(w1_rest_summed, 1)
                        pe.wait_ge(z_ready, 1)
                        for t in range(NAT1, XQ):
                            nc.tensor.matmul(y, w_raw[1][:, t, :], z[:, 0, t, :], start=False, stop=False)
                        nc.tensor.matmul(y, wq_raw[:, 1, :], z[:, 0, XQ, :], start=False, stop=False)
                        pe.wait_ge(zx0_ready, 1)
                        nc.tensor.matmul(y, w_raw[1][:, XQ, :], z[:, RING - 1, 0, :], start=False, stop=True
                                         ).then_inc(group_used, 1)
                        continue
                    if isinstance(i, int) and g == 0 and i == max(layer - 1, 1):
                        pe.wait_ge(w_split[layer], 1)
                    natives, splits = tile_places(layer)
                    if layer == 1:
                        pe.wait_ge(z_native_ready, i + 1)
                    else:
                        pe.wait_ge(z_ready, q + 1)
                    for t in range(native):
                        nc.tensor.matmul(y, w_raw[layer][:, natives.index((g, t)), :], z[:, slot, t, :],
                                         start=(g == 0 and t == 0), stop=False)
                    by_pool = end - native - QUARTER[layer]
                    places = [(t, splits.index((g, native + t))) for t in range(by_pool)]
                    x_part, x_weights = end - native, splits.index((g, GT - 1))
                    pe.wait_ge(zh_ready, q)
                    for t, w in places:
                        nc.tensor.matmul(y, wh[layer][:, w, :], zh[:, slot, t, :], start=False, stop=False)
                        nc.tensor.matmul(y, wl[layer][:, w, :], zh[:, slot, t, :], start=False, stop=False)
                    if layer == 1:
                        if i_is(i, 1):
                            pe.wait_ge(wq_made, 1)
                        nc.tensor.matmul(y, wq[:, 0, :], zh[:, slot, by_pool, :], start=False, stop=False)
                    if by_dve:
                        pe.wait_ge(zxh_ready, e + 1)
                        for weights in (wh, wl):
                            nc.tensor.matmul(y, weights[layer][:, x_weights, :], zh[:, slot, x_part, :],
                                             start=False, stop=False)
                    last = g == GROUPS[layer] - 1
                    pe.wait_ge(zl_ready, q)
                    for t, w in places:
                        end_here = last and not by_dve and not QUARTER[layer] and t == by_pool - 1
                        mm = nc.tensor.matmul(y, wh[layer][:, w, :], zl[:, slot, t, :], start=False, stop=end_here)
                    if layer == 1:
                        mm = nc.tensor.matmul(y, wq[:, 1, :], zl[:, slot, by_pool, :], start=False,
                                              stop=(last and not by_dve))
                    if by_dve:
                        pe.wait_ge(zxl_ready, e + 1)
                        mm = nc.tensor.matmul(y, wh[layer][:, x_weights, :], zl[:, slot, x_part, :],
                                              start=False, stop=last)
                    mm.then_inc(group_used, 1)

            iterate(pe, body, NCHUNK + 1)

            pe.wait_ge(pooled[3], NCHUNK)
            dot(pooled3, 4, slice(BATCH - SAMPLES, BATCH), False, True).then_inc(out_summed, 1)


def tiles_on_host(w, layer):
    native, split = tile_places(layer)
    return w[:, [g * GT + t for g, t in native + split], :]


def kernel(r_sparse_embed, L0_rec_W1, L0_rec_b1, L0_rec_W2, L0_rec_b2, L0_rec_W3, L0_rec_b3,
           L0_rec_Wo, L0_rec_bo):
    import numpy as np
    import concourse.bacc as bacc
    from concourse.bass_utils import run_bass_kernel_spmd as run

    x = np.asarray(r_sparse_embed).transpose(1, 0, 2).reshape(Q, N)
    roll = np.r_[HALF:P, 0:HALF]
    W1 = np.asarray(L0_rec_W1).reshape(P, Q, Q)
    h = np.arange(Q)[None, :, None]
    shift = (4 * np.arange(4)[None, None, :] + np.arange(4)[:, None, None])
    w1a = W1[:, h, (h + shift) % Q].transpose(1, 2, 3, 0).reshape(P, 4, P)
    w1b = W1[:, (h + shift) % Q, h].transpose(1, 2, 3, 0).reshape(P, 4, P)
    k = np.arange(Q)
    w1q = np.stack([np.tile(W1[:, k, (k + Q // 2) % Q].T, (4, 1))] * 2, axis=1)
    w1b[:Q, 0], w1q[2 * Q:, 0], w1q[Q:, 1] = 0, 0, 0

    def blocks(W, layer):
        w = np.asarray(W).reshape(P, 2, Q, 8, 4).transpose(4, 2, 1, 3, 0)
        w = np.stack([w[m][:, ::-1] if m % 2 else w[m] for m in range(4)])
        return tiles_on_host(w.reshape(P, 16, P), layer)

    Wo = np.asarray(L0_rec_Wo)[0]
    arrays = {
        "xt": np.concatenate([x, x[:Q // 2]]),
        "w1": np.concatenate([w1a[:, :NAT1], w1b[:, :NAT1], w1a[:, NAT1:], w1b[:, NAT1:], w1q], axis=1),
        "w2": blocks(np.asarray(L0_rec_W2)[roll], 2), "w3": blocks(L0_rec_W3, 3),
        "cols": np.stack([np.asarray(L0_rec_b1), np.asarray(L0_rec_b2)[roll], np.asarray(L0_rec_b3),
                          Wo[:P][roll], Wo[P:]], axis=1),
        "bo": np.asarray(L0_rec_bo).reshape(1, 1),
    }
    arrays = {f"{n}_dram": np.ascontiguousarray(a) for n, a in arrays.items()}
    nc = bacc.Bacc("TRN2", target_bir_lowering=False, num_devices=1)
    args = [nc.dram_tensor(n, a.shape, F32, kind="ExternalInput").ap() for n, a in arrays.items()]
    args.append(nc.dram_tensor("out_dram", (BATCH, 1), F32, kind="ExternalOutput").ap())
    cin_kernel(nc, *args)
    return run(nc, [arrays], core_ids=[0]).results[0]["out_dram"]
```

```python
from contextlib import ExitStack

import concourse.bass as bass
from concourse import mybir

F32 = mybir.dt.float32
F32R = mybir.dt.float32r
ALU = mybir.AluOpType
ACT = mybir.ActivationFunctionType
AX_X = mybir.AxisListType.X

P = 128
Q = 32
D = 16
BATCH = 512
N = BATCH * D
CH = 512
NCHUNK = N // CH
SAMPLES = CH // D
EARLY = BATCH - SAMPLES
HALF = 64
X_HALF = {1: slice(0, HALF), 2: slice(HALF, P)}
RESULTS = {1: slice(HALF, P), 2: slice(0, HALF), 3: slice(0, P)}
GT = 4
RING = 3
SPLIT = {1: (2,), 2: (3, 3, 3, 3), 3: (3, 3, 3, 3)}
BY_DVE = {1: (1,), 2: (1, 0, 1, 0), 3: (1, 0, 1, 0)}
ZX_BANK = {0: 1, 1: 0, 3: 1, 5: 0, 7: 1}
QUARTER = {1: 1, 2: 0, 3: 0}
PARTS = 3
ZT = 4
GROUPS = {layer: len(s) for layer, s in SPLIT.items()}
PER_ITER = sum(GROUPS.values())
DVE_PER_ITER = sum(n for by_dve in BY_DVE.values() for n in by_dve)
FIRST = {1: 0, 2: GROUPS[1], 3: GROUPS[1] + GROUPS[2]}
NATIVE_GROUPS = 3
NATIVE_CUT = 2
BSLOTS = 3
XSLOTS = 2
NAT1 = GT - SPLIT[1][0]
XT = GT + 1
XQ = GT - BY_DVE[1][0]
LOOP = (4, NCHUNK - 2)


def tile_places(layer):
    native = [(g, t) for g, s in enumerate(SPLIT[layer]) for t in range(GT - s)]
    split = [(g, t) for g, s in enumerate(SPLIT[layer]) for t in range(GT - s, GT)]
    return native, split


def split_part(layer, part):
    if layer == 1:
        return slice(0, sum(SPLIT[1]))
    middle = sum(SPLIT[layer][:GROUPS[layer] // 2])
    return (slice(0, middle), slice(middle, sum(SPLIT[layer])))[part]


def layers_of(i):
    return [layer for layer in (1, 2, 3) if 0 <= i - layer + 1 < NCHUNK]


def groups_before(i):
    if isinstance(i, int) and (i < 2 or i > NCHUNK):
        return sum(GROUPS[layer] for k in range(i) for layer in layers_of(k))
    return i * PER_ITER + (sum(GROUPS[layer] for k in range(2) for layer in layers_of(k)) - 2 * PER_ITER)


def dve_tiles_before(i):
    if isinstance(i, int) and (i < 2 or i > NCHUNK):
        return sum(by_dve for k in range(i) for *_, by_dve in dve_tiles(k))
    return i * DVE_PER_ITER + (sum(by_dve for k in range(2) for *_, by_dve in dve_tiles(k)) - 2 * DVE_PER_ITER)


def dve_tiles(i):
    order = [(layer, g) for layer in (1, 2, 3) if exists(i - (layer - 1)) for g in range(GROUPS[layer])]
    return [(layer, g, 0 if is_native(groups_before(i) + k) else BY_DVE[layer][g])
            for k, (layer, g) in enumerate(order)]


def groups_through(layer, c):
    i = c + layer - 1
    if isinstance(i, int):
        return groups_before(i) + sum(GROUPS[k] for k in layers_of(i) if k <= layer)
    return groups_before(i) + FIRST[layer] + GROUPS[layer]


def is_native(q):
    return isinstance(q, int) and q < NATIVE_GROUPS


def i_is(i, number):
    return isinstance(i, int) and i == number


def exists(chunk):
    return not isinstance(chunk, int) or 0 <= chunk < NCHUNK


def steps(i):
    found, q, e = [], groups_before(i), dve_tiles_before(i)
    for layer, g, by_dve in dve_tiles(i):
        found.append((FIRST[layer] + g, layer, g, q + len(found), e))
        e = e + by_dve
    return found


def parts_of(layer, g):
    by_dve = BY_DVE[layer][g]
    return GT - SPLIT[layer][g], GT + QUARTER[layer] - by_dve, by_dve


def slot_of(i, k):
    return (groups_before(i) + k) % RING if isinstance(i, int) else k % RING


assert groups_before(2) % RING == 0 and PER_ITER % RING == 0


def iterate(engine, body, last):
    for i in range(LOOP[0]):
        body(i)
    with engine.Fori(LOOP[0], LOOP[1]) as i:
        body(i)
    for i in range(LOOP[1], last + 1):
        body(i)


def cin_kernel(nc, xt, w1, w2, w3, cols, bo, out):
    with ExitStack() as ctx:
        def sb(name, shape, dt=F32):
            return ctx.enter_context(nc.sbuf_tensor(name, shape, dt))

        def sem(name):
            return ctx.enter_context(nc.semaphore(name))

        nat = {layer: len(tile_places(layer)[0]) for layer in (1, 2, 3)}
        spl = {layer: len(tile_places(layer)[1]) for layer in (1, 2, 3)}

        w1_sb = sb("w1_sb", [P, 2 * GT + 2, P])
        w_raw = {1: sb("w1_sum", [P, GT * GROUPS[1], P]), 2: sb("w2_raw", [P, GT * GROUPS[2], P]),
                 3: sb("w3_raw", [P, GT * GROUPS[3], P])}
        wh = {layer: sb(f"w{layer}_high", [P, spl[layer], P], F32R) for layer in (1, 2, 3)}
        wl = {layer: sb(f"w{layer}_low", [P, spl[layer], P], F32R) for layer in (1, 2, 3)}
        wq_raw = w1_sb[:, 2 * GT:, :]
        wq = sb("wq", [P, 2, P], F32R)
        cols_sb = sb("cols_sb", [P, 5])
        bo_sb = sb("bo_sb", [1, 1])

        x_rep = sb("x_rep", [P, XSLOTS * CH])
        shifted = sb("shifted", [P, XSLOTS * XT * CH])
        b_fac = sb("b_fac", [P, BSLOTS * 8 * CH])
        z = sb("z", [P, RING, ZT, CH])
        zh = sb("zh", [P, RING, PARTS, CH], F32R)
        zl = sb("zl", [P, RING, PARTS, CH], F32R)
        x_out = {layer: sb(f"x{layer}_sb", [P, CH]) for layer in (1, 2)}
        results12 = sb("results12", [P, CH])
        results3 = sb("results3", [P, CH])
        a_rep = {2: sb("a2_rep", [P, 2, CH]), 3: sb("a3_rep", [P, 2, CH])}
        z_fifth = (results3, x_out[2])
        pooled12 = sb("pooled12", [P, BATCH + SAMPLES])
        pooled3 = sb("pooled3", [P, BATCH])
        terms = sb("terms", [P, EARLY])
        ones = sb("ones", [P, 1])
        out_sb = sb("out_sb", [1, BATCH])

        def psum(name, shape):
            return ctx.enter_context(nc.psum_tensor(name, shape, F32))

        x_ps = psum("x_ps", [P, CH])
        a_ps = psum("a_ps", [P, 2, CH])
        zx_ps = psum("zx_ps", [P, 2, CH])
        y_ps = {layer: psum(f"y{layer}_ps", [P, CH]) for layer in (1, 2, 3)}

        w1_loaded = sem("w1_loaded")
        w1_rest_loaded = sem("w1_rest_loaded")
        w_loaded = {2: (sem("w2_loaded"), sem("w2_rest_loaded")),
                    3: (sem("w3_loaded"), sem("w3_rest_loaded"))}
        cols_loaded = sem("cols_loaded")
        bo_loaded = sem("bo_loaded")
        w1_summed = sem("w1_summed")
        w1_rest_summed = sem("w1_rest_summed")
        w_rounded = {layer: sem(f"w{layer}_rounded") for layer in (1, 2, 3)}
        w_split = {layer: sem(f"w{layer}_split") for layer in (1, 2, 3)}
        wq_rounded = sem("wq_rounded")
        wq_made = sem("wq_made")
        x0_loaded = (sem("x0_native_loaded"), sem("x0_rest_loaded"))
        x_loaded = (sem("x_native_loaded"), sem("x_rest_loaded"))
        b0_loaded = (sem("b0_loaded"), sem("b0_rest_loaded"))
        b_loaded = sem("b_loaded")
        x_in_psum = sem("x_in_psum")
        a_spread = {2: (sem("a2_0_spread"), sem("a2_1_spread")),
                    3: (sem("a3_0_spread"), sem("a3_1_spread"))}
        a_in_psum = {2: (sem("a2_0_in_psum"), sem("a2_1_in_psum")),
                     3: (sem("a3_0_in_psum"), sem("a3_1_in_psum"))}
        z_native_ready = sem("z_native_ready")
        z_ready = sem("z_ready")
        zh_ready = sem("zh_ready")
        zl_ready = sem("zl_ready")
        zx_ready = sem("zx_ready")
        zxh_ready = sem("zxh_ready")
        zxl_ready = sem("zxl_ready")
        z_fifth_ready = sem("z_fifth_ready")
        group_used = sem("group_used")
        x_ready = {layer: sem(f"x{layer}_ready") for layer in (1, 2)}
        results_ready = {layer: sem(f"results{layer}_ready") for layer in (1, 2, 3)}
        pooled12_done = sem("pooled12_done")
        pooled3_done = sem("pooled3_done")
        ones_set = sem("ones_set")
        terms_made = sem("terms_made")
        last_begun = sem("last_begun")
        out_summed = sem("out_summed")
        out_ready = sem("out_ready")
        out_stored = sem("out_stored")
        X_DMAS, B_DMAS, A_DMAS = 3, 4, (2, 3)

        def bank(layer, c):
            return y_ps[2] if layer == 3 and i_is(c, NCHUNK - 1) else y_ps[layer]

        block = ctx.enter_context(nc.Block())

        @block.sync
        def _(sp):
            def load_x(c, parts=(0, 1)):
                if not isinstance(c, int) or c > 1:
                    for part in parts:
                        sp.wait_ge(x_loaded[part], (c - 1) * (16 * X_DMAS))
                n = bass.ds(c * CH, CH)
                slot = c % XSLOTS
                loaded = x0_loaded if i_is(c, 0) else x_loaded
                if 0 in parts:
                    sp.dma_start(x_rep[:, bass.ds(slot * CH, CH)], xt[0:Q, n].partition_broadcast(P // Q)
                                 ).then_inc(loaded[0], 16)
                for t in range(GT):
                    part = 0 if t < NAT1 else 1
                    if part in parts:
                        src = bass.AP(xt.tensor, 4 * t * N, [[N, 4], [N, Q], [1, N]])
                        place = t if t < XQ else t + 1
                        sp.dma_start(shifted[:, bass.ds(slot * (XT * CH) + place * CH, CH)], src[:, :, n]
                                     ).then_inc(loaded[part], 16)
                if 1 in parts:
                    sp.dma_start(shifted[:, bass.ds(slot * (XT * CH) + XQ * CH, CH)],
                                 xt[Q // 2:Q // 2 + Q, n].partition_broadcast(P // Q)
                                 ).then_inc(loaded[1], 16)

            def load_b(c, parts=None):
                if not isinstance(c, int) or c > 1:
                    sp.wait_ge(b_loaded, (c - 1) * (16 * B_DMAS))
                if not isinstance(c, int) or c >= BSLOTS:
                    sp.wait_ge(z_native_ready, groups_before(c))
                for j, end, loaded in parts or ((0, 8, b_loaded),):
                    size = (end - j) * CH
                    dst = b_fac[:, bass.ds((c % BSLOTS) * (8 * CH) + j * CH, size)
                                ].rearrange("p (j n) -> p j n", j=end - j)
                    for m in range(4):
                        src = bass.AP(xt.tensor, (4 * j + m) * N, [[0, Q], [4 * N, end - j], [1, N]])
                        sp.dma_start(dst[Q * m:Q * m + Q], src[:, :, bass.ds(c * CH, CH)]).then_inc(loaded, 16)

            def spread(layer, c):
                sp.wait_ge(x_ready[layer], c + 1)
                top = X_HALF[layer].start
                for k, to, rows, count in ((0, 0, 0, 2), (0, 2, 0, 2), (1, 1, 0, 2), (1, 3, 0, 1), (1, 0, 1, 1)):
                    sp.dma_start(a_rep[layer + 1][Q * to:Q * (to + count), k, :],
                                 x_out[layer][top + Q * rows:top + Q * (rows + count), :]
                                 ).then_inc(a_spread[layer + 1][k], 16)

            def load_w(layer, w, part):
                middle = nat[layer] + split_part(layer, 0).stop
                tiles = slice(0, middle) if part == 0 else slice(middle, GT * GROUPS[layer])
                sp.dma_start(w_raw[layer][:, tiles, :], w[:, tiles, :]).then_inc(w_loaded[layer][part], 16)

            load_x(0, (0,))
            sp.dma_start(w1_sb[:, 0:2 * NAT1], w1[:, 0:2 * NAT1]).then_inc(w1_loaded, 16)
            load_x(0, (1,))
            sp.dma_start(w1_sb[:, 2 * NAT1:], w1[:, 2 * NAT1:]).then_inc(w1_rest_loaded, 16)
            sp.dma_start(cols_sb[:], cols).then_inc(cols_loaded, 16)
            load_x(1)
            load_w(2, w2, 0)
            load_b(0, ((0, 4, b0_loaded[0]),))

            def body(i):
                if exists(i):
                    spread(1, i)
                if i_is(i, 0):
                    load_b(0, ((4, 8, b0_loaded[1]),))
                    load_w(2, w2, 1)
                if i_is(i, 1):
                    load_w(3, w3, 0)
                    load_w(3, w3, 1)
                if exists(i + 2):
                    load_x(i + 2)
                if exists(i - 1):
                    spread(2, i - 1)
                if exists(i + 1):
                    load_b(i + 1)
                if i_is(i, 0):
                    sp.dma_start(bo_sb[:], bo).then_inc(bo_loaded, 16)

            iterate(sp, body, NCHUNK)
            sp.wait_ge(out_ready, 2)
            sp.dma_start(out.rearrange("b o -> o b"), out_sb[:]).then_inc(out_stored, 16)
            sp.wait_ge(out_stored, 16)

        @block.scalar
        def _(act):
            def x_to_psum(c):
                act.wait_ge(x_loaded[0], c * (16 * X_DMAS))
                nc.scalar.activation(x_ps[:], x_rep[:, bass.ds((c % XSLOTS) * CH, CH)], ACT.Copy
                                     ).then_inc(x_in_psum, 1)

            def a_to_psum(layer, half, c):
                act.wait_ge(a_spread[layer][half], (c + 1) * (16 * A_DMAS[half]))
                nc.scalar.activation(a_ps[:, half, :], a_rep[layer][:, half, :], ACT.Copy
                                     ).then_inc(a_in_psum[layer][half], 1)

            def y_to_sbuf(layer, c):
                act.wait_ge(group_used, groups_through(layer, c))
                if i_is(c, 0) and layer == 1:
                    act.wait_ge(cols_loaded, 16)
                if layer < 3:
                    x = X_HALF[layer]
                    nc.scalar.activation(x_out[layer][x, :], bank(layer, c)[x, :], ACT.Relu,
                                         bias=cols_sb[x, layer - 1:layer]).then_inc(x_ready[layer], 1)
                results, rows = (results12, results12, results3)[layer - 1], RESULTS[layer]
                if layer == 2:
                    act.wait_ge(pooled12_done, c + 1)
                elif not isinstance(c, int) or c > 0:
                    act.wait_ge(pooled12_done if layer == 1 else pooled3_done, c)
                nc.scalar.activation(results[rows, :], bank(layer, c)[rows, :], ACT.Relu,
                                     bias=cols_sb[rows, layer - 1:layer]).then_inc(results_ready[layer], 1)

            def round_w(layer, part):
                if layer > 1:
                    act.wait_ge(w_loaded[layer][part], 16)
                tiles = split_part(layer, part)
                nc.scalar.activation(wh[layer][:, tiles, :], w_raw[layer][:, nat[layer]:, :][:, tiles, :], ACT.Copy
                                     ).then_inc(w_rounded[layer], 1)

            act.wait_ge(w1_rest_summed, 1)
            nc.scalar.activation(wq[:], wq_raw, ACT.Copy).then_inc(wq_rounded, 1)
            round_w(1, 0)

            def body(i):
                here = {step[0]: (step, k) for k, step in enumerate(steps(i))}
                for pos in range(PER_ITER):
                    if pos in here and not is_native(here[pos][0][3]):
                        (pos, layer, g, q, e), k = here[pos]
                        slot, (native, end, by_dve) = slot_of(i, k), parts_of(layer, g)
                        act.wait_ge(z_ready, q + 1)
                        nc.scalar.activation(zh[:, slot, 0:end - native, :], z[:, slot, native:end, :], ACT.Copy
                                             ).then_inc(zh_ready, 1)
                        if by_dve:
                            act.wait_ge(zx_ready, e + 1)
                            nc.scalar.activation(zh[:, slot, end - native, :], zx_ps[:, ZX_BANK[pos], :], ACT.Copy
                                                 ).then_inc(zxh_ready, 1)
                    if pos == 0 and i_is(i, 0):
                        y_to_sbuf(1, 0)
                    if pos == 0 and i_is(i, 1):
                        round_w(2, 0)
                        a_to_psum(2, 0, 0)
                        a_to_psum(2, 1, 0)
                        round_w(2, 1)
                    if pos == 4 and i_is(i, 1):
                        a_to_psum(2, 0, 1)
                    if pos == 0 and i_is(i, 2):
                        y_to_sbuf(2, 0)
                    if pos in (2, 4) and i_is(i, 2):
                        round_w(3, pos // 2 - 1)
                    if pos == 0 and i_is(i, NCHUNK):
                        act.wait_ge(z_native_ready, groups_before(i))
                    if pos == 0 and exists(i - 1) and not i_is(i, 1):
                        a_to_psum(2, 1, i - 1)
                    if pos == 3 and exists(i - 2):
                        a_to_psum(3, 0, i - 2)
                    if pos == 5 and exists(i - 2):
                        a_to_psum(3, 1, i - 2)
                    if pos == (6 if i_is(i, NCHUNK + 1) else 3) and exists(i - 3):
                        y_to_sbuf(3, i - 3)
                    if pos == (2 if i_is(i, 1) else 4) and exists(i) and not i_is(i, 0):
                        y_to_sbuf(1, i)
                    if pos == (3 if i_is(i, 1) else 5) and exists(i + 1) and not i_is(i, 0):
                        x_to_psum(i + 1)
                    if pos == 7 and exists(i) and not i_is(i, 0) and not i_is(i, 1):
                        a_to_psum(2, 0, i)
                    if pos == (6 if i_is(i, NCHUNK) else 7) and exists(i - 1) and not i_is(i, 1):
                        y_to_sbuf(2, i - 1)

            iterate(act, body, NCHUNK + 2)

        @block.gpsimd
        def _(pool):
            nc.gpsimd.memset(ones[:], 1.0).then_inc(ones_set, 1)
            pool.wait_ge(w1_rest_loaded, 16)
            nc.gpsimd.tensor_tensor(w_raw[1][:, NAT1:, :], w1_sb[:, 2 * NAT1:GT + NAT1, :],
                                    w1_sb[:, GT + NAT1:2 * GT, :], ALU.add).then_inc(w1_rest_summed, 1)

            def body(i):
                for k, (pos, layer, g, q, e) in enumerate(steps(i)):
                    if is_native(q):
                        continue
                    slot, (native, end, by_dve) = slot_of(i, k), parts_of(layer, g)
                    pool.wait_ge(zh_ready, q - NATIVE_GROUPS + 1)
                    nc.gpsimd.tensor_tensor(zl[:, slot, 0:end - native, :], z[:, slot, native:end, :],
                                            zh[:, slot, 0:end - native, :].bitcast(F32), ALU.subtract
                                            ).then_inc(zl_ready, 1)

            iterate(pool, body, NCHUNK + 1)

        @block.vector
        def _(dve):
            def split_w(layer, part):
                dve.wait_ge(w_rounded[layer], part + 1)
                tiles = split_part(layer, part)
                nc.vector.tensor_tensor(wl[layer][:, tiles, :], w_raw[layer][:, nat[layer]:, :][:, tiles, :],
                                        wh[layer][:, tiles, :].bitcast(F32), ALU.subtract).then_inc(w_split[layer], 1)

            def pool_dims(results, pooled, rows, block):
                return nc.vector.tensor_reduce(pooled[rows, bass.ds(block * SAMPLES, SAMPLES)],
                                               results[rows, :].rearrange("p (b d) -> p b d", d=D),
                                               AX_X, ALU.add)

            def pool12(i):
                if exists(i):
                    dve.wait_ge(results_ready[1], i + 1)
                if exists(i - 1):
                    dve.wait_ge(results_ready[2], i)
                rows = RESULTS[1] if i_is(i, 0) else RESULTS[2] if i_is(i, NCHUNK) else slice(0, P)
                pool_dims(results12, pooled12, rows, i).then_inc(pooled12_done, 1)

            def early_samples():
                dve.wait_ge(cols_loaded, 16)
                dve.wait_ge(pooled3_done, NCHUNK - 1)
                nc.vector.tensor_scalar(terms[:], pooled3[:, 0:EARLY], cols_sb[:, 4:5], None, ALU.mult
                                        ).then_inc(terms_made, 1)
                dve.wait_ge(pooled12_done, NCHUNK + 1)
                dve.wait_ge(terms_made, 1)
                for rows, first in ((RESULTS[1], 0), (RESULTS[2], SAMPLES)):
                    nc.vector.scalar_tensor_tensor(terms[rows, :], pooled12[rows, first:first + EARLY],
                                                   cols_sb[rows, 3:4], terms[rows, :], ALU.mult, ALU.add
                                                   ).then_inc(terms_made, 1)
                dve.wait_ge(out_summed, 1)
                dve.wait_ge(bo_loaded, 16)
                nc.vector.tensor_scalar(out_sb[:, 0:EARLY], y_ps[1][0:1, 0:EARLY], bo_sb[0:1, 0:1], None, ALU.add
                                        ).then_inc(out_ready, 1)

            def pool3(c):
                dve.wait_ge(results_ready[3], c + 1)
                pool_dims(results3, pooled3, RESULTS[3], c).then_inc(pooled3_done, 1)

            def multiply(dst, factor, others):
                return nc.vector.tensor_tensor(dst, factor.unsqueeze(1).to_broadcast(list(dst.shape)), others,
                                               ALU.mult)

            def product(i, step, k):
                pos, layer, g, q, e = step
                c, slot, (native, end, by_dve) = i - (layer - 1), slot_of(i, k), parts_of(layer, g)
                if layer == 1:
                    others = shifted[:, bass.ds((c % XSLOTS) * (XT * CH), XT * CH)
                                     ].rearrange("p (t n) -> p t n", t=XT)
                    if is_native(q):
                        factor = x_rep[:, c * CH:(c + 1) * CH]
                        dve.wait_ge((x0_loaded, x_loaded)[c][0], 16 * X_DMAS)
                    else:
                        factor = x_ps[:]
                        dve.wait_ge(x_in_psum, c - 1)
                        dve.wait_ge(x_loaded[1], c * (16 * X_DMAS))
                else:
                    half, j = divmod(g, GROUPS[layer] // 2)
                    others = b_fac[:, bass.ds((c % BSLOTS) * (8 * CH) + GT * j * CH, GT * CH)
                                   ].rearrange("p (j n) -> p j n", j=GT)
                    if layer == 2 and i_is(c, 0):
                        dve.wait_ge(b0_loaded[j], 16 * B_DMAS)
                    elif layer == 2 and g == 0:
                        dve.wait_ge(b_loaded, c * (16 * B_DMAS))
                    if is_native(q):
                        factor = a_rep[layer][:, half, :]
                        dve.wait_ge(a_spread[layer][half], 16 * A_DMAS[half])
                    else:
                        factor = a_ps[:, half, :]
                        dve.wait_ge(a_in_psum[layer][half], c + 1)
                if not isinstance(q, int) or q >= RING:
                    dve.wait_ge(group_used, q - (RING - 1))

                if is_native(q):
                    multiply(z[:, slot, 0:NATIVE_CUT, :], factor, others[:, 0:NATIVE_CUT, :]
                             ).then_inc(z_native_ready, 1)
                    if i_is(i, 0):
                        dve.wait_ge(w1_loaded, 16)
                        nc.vector.tensor_tensor(w_raw[1][:, 0:NAT1, :], w1_sb[:, 0:NAT1, :],
                                                w1_sb[:, NAT1:2 * NAT1, :], ALU.add).then_inc(w1_summed, 1)
                    if layer == 1:
                        dve.wait_ge((x0_loaded, x_loaded)[c][1], 16 * X_DMAS)
                    multiply(z[:, slot, NATIVE_CUT:, :], factor, others[:, NATIVE_CUT:GT, :]).then_inc(z_ready, 1)
                    if layer == 1:
                        multiply(z_fifth[c][:].unsqueeze(1), factor, others[:, GT:, :]).then_inc(z_fifth_ready, 1)
                    return

                multiply(z[:, slot, native:end, :], factor, others[:, native:end, :]).then_inc(z_ready, 1)
                if by_dve:
                    done = e - 1 if pos == 1 else e
                    if not isinstance(e, int) or done > 0:
                        dve.wait_ge(zxl_ready, done)
                    bank = ZX_BANK[pos]
                    multiply(zx_ps[:, bank:bank + 1, :], factor, others[:, end:, :]).then_inc(zx_ready, 1)
                multiply(z[:, slot, 0:native, :], factor, others[:, 0:native, :]).then_inc(z_native_ready, 1)

            def subtract(i, step, k):
                pos, layer, g, q, e = step
                slot, (native, end, by_dve) = slot_of(i, k), parts_of(layer, g)
                dve.wait_ge(zxh_ready, e + 1)
                nc.vector.tensor_tensor(zl[:, slot, end - native, :], zx_ps[:, ZX_BANK[pos], :],
                                        zh[:, slot, end - native, :].bitcast(F32), ALU.subtract
                                        ).then_inc(zxl_ready, 1)

            def body(i):
                here = {s[0]: (s, k) for k, s in enumerate(steps(i))}
                for pos in range(PER_ITER):
                    if pos in here:
                        product(i, *here[pos])
                    if pos - 1 in here and pos - 1 in ZX_BANK and not is_native(here[pos - 1][0][3]):
                        subtract(i, *here[pos - 1])
                    if pos == 0 and i_is(i, 0):
                        dve.wait_ge(wq_rounded, 1)
                        nc.vector.tensor_tensor(wq[Q:2 * Q, 0, :], wq_raw[Q:2 * Q, 0, :],
                                                wq[Q:2 * Q, 0, :].bitcast(F32), ALU.subtract).then_inc(wq_made, 1)
                        split_w(1, 0)
                    if pos in (0, 2) and i_is(i, 1):
                        split_w(2, pos // 2)
                    if pos in (3, 5) and i_is(i, 2):
                        split_w(3, pos // 2 - 1)
                    if pos == (2 if i_is(i, 2) else 1) and (exists(i - 1) or i_is(i, NCHUNK + 1)):
                        pool12(i - 1)
                    if pos == (7 if i_is(i, NCHUNK + 1) else 5) and exists(i - 3):
                        pool3(i - 3)
                    if pos == 8 and i_is(i, NCHUNK + 1):
                        early_samples()

            iterate(dve, body, NCHUNK + 2)
            dve.wait_ge(out_summed, 2)
            nc.vector.tensor_scalar(out_sb[:, EARLY:], y_ps[3][0:1, 0:SAMPLES], bo_sb[0:1, 0:1], None, ALU.add
                                    ).then_inc(out_ready, 1)

        @block.tensor
        def _(pe):
            def dot(column, rows, part, first, start=False, stop=False):
                return nc.tensor.matmul(y_ps[3][0:1, 0:SAMPLES], cols_sb[rows, column:column + 1],
                                        part[rows, first:first + SAMPLES], start=start, stop=stop)

            def body(i):
                for k, (pos, layer, g, q, e) in enumerate(steps(i)):
                    if i_is(i, NCHUNK + 1) and g == GROUPS[3] - 1:
                        pe.wait_ge(ones_set, 1)
                        pe.wait_ge(terms_made, 3)
                        nc.tensor.matmul(y_ps[1][0:1, 0:EARLY], ones[:], terms[:], start=True, stop=True
                                         ).then_inc(out_summed, 1)
                        pe.wait_ge(pooled12_done, NCHUNK + 1)
                        pe.wait_ge(results_ready[3], NCHUNK - 1)
                        dot(3, RESULTS[1], pooled12, EARLY, start=True).then_inc(last_begun, 1)
                        pe.wait_ge(last_begun, 1)
                        dot(3, RESULTS[2], pooled12, EARLY + SAMPLES)
                    c, slot, (native, end, by_dve) = i - (layer - 1), slot_of(i, k), parts_of(layer, g)
                    y = bank(layer, c)[:]
                    if g == 0 and layer == 3 and i_is(c, NCHUNK - 1):
                        pe.wait_ge(results_ready[2], NCHUNK)
                    elif g == 0 and (not isinstance(c, int) or c > 0):
                        pe.wait_ge(results_ready[layer], c)
                    natives, splits = tile_places(layer)
                    if is_native(q):
                        if layer == 1:
                            pe.wait_ge(w1_summed, 1)
                        else:
                            pe.wait_ge(w_loaded[layer][0], 16)
                        pe.wait_ge(z_native_ready, q + 1)
                        for t in range(GT):
                            if t == NATIVE_CUT:
                                if layer == 1:
                                    pe.wait_ge(w1_rest_summed, 1)
                                pe.wait_ge(z_ready, q + 1)
                            if layer == 1 and t == XQ:
                                weights = wq_raw[:, 1, :]
                            else:
                                weights = w_raw[layer][:, (natives + splits).index((g, t)), :]
                            mm = nc.tensor.matmul(y, weights, z[:, slot, t, :], start=(g == 0 and t == 0), stop=False)
                        if layer == 1:
                            pe.wait_ge(z_fifth_ready, c + 1)
                            mm = nc.tensor.matmul(y, w_raw[1][:, XQ, :], z_fifth[c][:], start=False, stop=True)
                        mm.then_inc(group_used, 1)
                        continue
                    if i_is(i, 2) and layer == 1:
                        pe.wait_ge(w_split[1], 1)
                        pe.wait_ge(wq_made, 1)
                    for part, first in enumerate((1 if layer == 2 else 0, 2)):
                        if layer > 1 and i_is(i, layer - 1) and g == first:
                            pe.wait_ge(w_split[layer], part + 1)

                    by_pool = end - native - QUARTER[layer]
                    places = [(t, splits.index((g, native + t))) for t in range(by_pool)]
                    x_part, x_weights = end - native, splits.index((g, GT - 1))
                    pe.wait_ge(zh_ready, q - NATIVE_GROUPS + 1)
                    for t, w in places:
                        nc.tensor.matmul(y, wh[layer][:, w, :], zh[:, slot, t, :],
                                         start=(g == 0 and t == 0), stop=False)
                        nc.tensor.matmul(y, wl[layer][:, w, :], zh[:, slot, t, :], start=False, stop=False)
                    if layer == 1:
                        nc.tensor.matmul(y, wq[:, 0, :], zh[:, slot, by_pool, :], start=False, stop=False)
                    if by_dve:
                        pe.wait_ge(zxh_ready, e + 1)
                        for weights in (wh, wl):
                            nc.tensor.matmul(y, weights[layer][:, x_weights, :], zh[:, slot, x_part, :],
                                             start=False, stop=False)
                    pe.wait_ge(z_native_ready, q + 1)
                    for t in range(native):
                        nc.tensor.matmul(y, w_raw[layer][:, natives.index((g, t)), :], z[:, slot, t, :],
                                         start=False, stop=False)
                    last = g == GROUPS[layer] - 1
                    pe.wait_ge(zl_ready, q - NATIVE_GROUPS + 1)
                    for t, w in places:
                        end_here = last and not by_dve and not QUARTER[layer] and t == by_pool - 1
                        mm = nc.tensor.matmul(y, wh[layer][:, w, :], zl[:, slot, t, :], start=False, stop=end_here)
                    if layer == 1:
                        mm = nc.tensor.matmul(y, wq[:, 1, :], zl[:, slot, by_pool, :], start=False,
                                              stop=(last and not by_dve))
                    if by_dve:
                        pe.wait_ge(zxl_ready, e + 1)
                        mm = nc.tensor.matmul(y, wh[layer][:, x_weights, :], zl[:, slot, x_part, :],
                                              start=False, stop=last)
                    mm.then_inc(group_used, 1)

            iterate(pe, body, NCHUNK + 1)

            pe.wait_ge(pooled3_done, NCHUNK)
            dot(4, RESULTS[3], pooled3, EARLY, stop=True).then_inc(out_summed, 1)


def tiles_on_host(w, layer):
    native, split = tile_places(layer)
    return w[:, [g * GT + t for g, t in native + split], :]


def kernel(r_sparse_embed, L0_rec_W1, L0_rec_b1, L0_rec_W2, L0_rec_b2, L0_rec_W3, L0_rec_b3,
           L0_rec_Wo, L0_rec_bo):
    import numpy as np
    import concourse.bacc as bacc
    from concourse.bass_utils import run_bass_kernel_spmd as run

    x = np.asarray(r_sparse_embed).transpose(1, 0, 2).reshape(Q, N)
    roll = np.r_[HALF:P, 0:HALF]
    W1 = np.asarray(L0_rec_W1).reshape(P, Q, Q)
    h = np.arange(Q)[None, :, None]
    shift = (4 * np.arange(4)[None, None, :] + np.arange(4)[:, None, None])
    w1a = W1[:, h, (h + shift) % Q].transpose(1, 2, 3, 0).reshape(P, 4, P)
    w1b = W1[:, (h + shift) % Q, h].transpose(1, 2, 3, 0).reshape(P, 4, P)
    k = np.arange(Q)
    w1q = np.stack([np.tile(W1[:, k, (k + Q // 2) % Q].T, (4, 1))] * 2, axis=1)
    w1b[:Q, 0], w1q[2 * Q:, 0], w1q[Q:, 1] = 0, 0, 0

    def blocks(W, layer):
        w = np.asarray(W).reshape(P, 2, Q, 8, 4).transpose(4, 2, 1, 3, 0)
        w = np.stack([w[m][:, ::-1] if m % 2 else w[m] for m in range(4)])
        return tiles_on_host(w.reshape(P, 16, P), layer)

    Wo = np.asarray(L0_rec_Wo)[0]
    arrays = {
        "xt": np.concatenate([x, x[:Q // 2]]),
        "w1": np.concatenate([w1a[:, :NAT1], w1b[:, :NAT1], w1a[:, NAT1:], w1b[:, NAT1:], w1q], axis=1),
        "w2": blocks(np.asarray(L0_rec_W2)[roll], 2), "w3": blocks(L0_rec_W3, 3),
        "cols": np.stack([np.asarray(L0_rec_b1), np.asarray(L0_rec_b2)[roll], np.asarray(L0_rec_b3),
                          Wo[:P][roll], Wo[P:]], axis=1),
        "bo": np.asarray(L0_rec_bo).reshape(1, 1),
    }
    arrays = {f"{n}_dram": np.ascontiguousarray(a) for n, a in arrays.items()}
    nc = bacc.Bacc("TRN2", target_bir_lowering=False, num_devices=1)
    args = [nc.dram_tensor(n, a.shape, F32, kind="ExternalInput").ap() for n, a in arrays.items()]
    args.append(nc.dram_tensor("out_dram", (BATCH, 1), F32, kind="ExternalOutput").ap())
    cin_kernel(nc, *args)
    return run(nc, [arrays], core_ids=[0]).results[0]["out_dram"]
```
